# Optimizing a Trainium2 kernel written in Bass

```python
import numpy as np
import jax
import jax.numpy as jnp

def _softmax(x, axis=-1):
    return jax.nn.softmax(x, axis=axis)

def _gelu(x):
    return jax.nn.gelu(x, approximate=True)

def _silu(x):
    return jax.nn.silu(x)

def _sigmoid(x):
    return jax.nn.sigmoid(x)

def _layernorm(x, axis=-1, eps=1e-05):
    m = jnp.mean(x, axis=axis, keepdims=True)
    v = jnp.var(x, axis=axis, keepdims=True)
    return (x - m) / jnp.sqrt(v + eps)

def _scatter_add(tgt, idx, src, axis=0):
    return tgt.at[idx].add(src)

def _segment_sum(src, seg, n):
    return jax.ops.segment_sum(src, seg, n)
kernel_name = 'mk_rec_standalone_d1_rec_r8_598693'

def setup_inputs(seed: int=0):
    np.random.seed(seed)
    _w = jnp.asarray

    def _rec_inputs():
        import jax
        import jax.numpy as jnp
        _rk = jax.random.key(seed)
        r_user_embeddings = -0.000928989 + 1.00043 * jax.random.normal(jax.random.fold_in(_rk, 1), (2048, 64), jnp.float32)
        r_price_features = 0.00513981 + 1.0024 * jax.random.normal(jax.random.fold_in(_rk, 2), (2048, 2), jnp.float32)
        r_temporal_features = -0.0043416 + 0.998921 * jax.random.normal(jax.random.fold_in(_rk, 3), (2048, 2), jnp.float32)
        r_item_ids = jax.random.randint(jax.random.fold_in(_rk, 4), (2048,), 26, 999969, jnp.int32)
        r_category_ids = jax.random.randint(jax.random.fold_in(_rk, 5), (2048,), 0, 1001, jnp.int32)
        r_wf1 = jax.random.randint(jax.random.fold_in(_rk, 6), (2048,), 0, 1250, jnp.int32)
        r_wf2 = jax.random.randint(jax.random.fold_in(_rk, 7), (2048,), 0, 9999, jnp.int32)
        return (r_user_embeddings, r_price_features, r_temporal_features, r_item_ids, r_category_ids, r_wf1, r_wf2)
    r_user_embeddings, r_price_features, r_temporal_features, r_item_ids, r_category_ids, r_wf1, r_wf2 = _rec_inputs()

    def _L0_rec_setup():
        import jax, jax.numpy as jnp
        import numpy as np
        B = 2048
        NUM_ITEMS = 125000
        NUM_CATS = 1001
        USER_DIM = 64
        ITEM_DIM = 64
        CAT_DIM = 32
        DIM1 = 1250
        DIM2 = 1250
        DEEP_IN = USER_DIM + ITEM_DIM + CAT_DIM + 2 + 2
        HID = [128, 64, 32]
        BN_EPS = 1e-05

        def _bn(x, g, b):
            return x * (g / jnp.sqrt(1.0 + BN_EPS)) + b
        key = jax.random.key(seed)
        ks = jax.random.split(key, 24)
        inp = {'user_embeddings': jax.random.normal(ks[0], (B, USER_DIM), jnp.float32), 'price_features': jax.random.normal(ks[1], (B, 2), jnp.float32), 'temporal_features': jax.random.normal(ks[2], (B, 2), jnp.float32), 'item_emb': jax.random.normal(ks[3], (NUM_ITEMS, ITEM_DIM), jnp.float32) * 0.02, 'cat_emb': jax.random.normal(ks[4], (NUM_CATS, CAT_DIM), jnp.float32) * 0.02, 'wide_emb1': jax.random.normal(ks[5], (DIM1, 1), jnp.float32) * 0.02, 'wide_emb2': jax.random.normal(ks[6], (DIM2, 1), jnp.float32) * 0.02, 'cross_W': jax.random.normal(ks[7], (DIM1 * DIM2,), jnp.float32) * 0.001, 'item_ids': jax.random.randint(ks[8], (B,), 0, NUM_ITEMS), 'category_ids': jax.random.randint(ks[9], (B,), 0, NUM_CATS), 'wf1': jax.random.randint(ks[10], (B,), 0, DIM1), 'wf2': jax.random.randint(ks[11], (B,), 0, DIM2)}
        dims = [DEEP_IN] + HID + [1]
        for i in range(4):
            fan_in = dims[i]
            inp[f'W{i + 1}'] = jax.random.normal(ks[12 + i], (dims[i], dims[i + 1]), jnp.float32) / np.sqrt(fan_in)
            inp[f'b{i + 1}'] = jnp.zeros((dims[i + 1],), jnp.float32)
        for i in range(3):
            inp[f'g{i + 1}'] = jnp.ones((HID[i],), jnp.float32)
            inp[f'be{i + 1}'] = jnp.zeros((HID[i],), jnp.float32)
        return inp
    _L0_rec_all = _L0_rec_setup()
    _L0_rec_in = {k: v for k, v in _L0_rec_all.items() if k in ('item_emb', 'cat_emb', 'wide_emb1', 'wide_emb2', 'cross_W', 'W1', 'b1', 'W2', 'b2', 'W3', 'b3', 'W4', 'b4', 'g1', 'be1', 'g2', 'be2', 'g3', 'be3')}
    del _L0_rec_all
    return {'r_user_embeddings': r_user_embeddings, 'r_price_features': r_price_features, 'r_temporal_features': r_temporal_features, 'r_item_ids': r_item_ids, 'r_category_ids': r_category_ids, 'r_wf1': r_wf1, 'r_wf2': r_wf2, 'L0_rec_item_emb': _L0_rec_in['item_emb'], 'L0_rec_cat_emb': _L0_rec_in['cat_emb'], 'L0_rec_wide_emb1': _L0_rec_in['wide_emb1'], 'L0_rec_wide_emb2': _L0_rec_in['wide_emb2'], 'L0_rec_cross_W': _L0_rec_in['cross_W'], 'L0_rec_W1': _L0_rec_in['W1'], 'L0_rec_b1': _L0_rec_in['b1'], 'L0_rec_W2': _L0_rec_in['W2'], 'L0_rec_b2': _L0_rec_in['b2'], 'L0_rec_W3': _L0_rec_in['W3'], 'L0_rec_b3': _L0_rec_in['b3'], 'L0_rec_W4': _L0_rec_in['W4'], 'L0_rec_b4': _L0_rec_in['b4'], 'L0_rec_g1': _L0_rec_in['g1'], 'L0_rec_be1': _L0_rec_in['be1'], 'L0_rec_g2': _L0_rec_in['g2'], 'L0_rec_be2': _L0_rec_in['be2'], 'L0_rec_g3': _L0_rec_in['g3'], 'L0_rec_be3': _L0_rec_in['be3']}

def reference(r_user_embeddings, r_price_features, r_temporal_features, r_item_ids, r_category_ids, r_wf1, r_wf2, L0_rec_item_emb, L0_rec_cat_emb, L0_rec_wide_emb1, L0_rec_wide_emb2, L0_rec_cross_W, L0_rec_W1, L0_rec_b1, L0_rec_W2, L0_rec_b2, L0_rec_W3, L0_rec_b3, L0_rec_W4, L0_rec_b4, L0_rec_g1, L0_rec_be1, L0_rec_g2, L0_rec_be2, L0_rec_g3, L0_rec_be3):
    import jax
    import jax.numpy as jnp

    def _L0_rec_ref(user_embeddings, price_features, temporal_features, item_emb, cat_emb, wide_emb1, wide_emb2, cross_W, W1, b1, W2, b2, W3, b3, W4, b4, g1, be1, g2, be2, g3, be3, item_ids, category_ids, wf1, wf2):
        import jax, jax.numpy as jnp
        import numpy as np
        B = 2048
        NUM_ITEMS = 125000
        NUM_CATS = 1001
        USER_DIM = 64
        ITEM_DIM = 64
        CAT_DIM = 32
        DIM1 = 1250
        DIM2 = 1250
        DEEP_IN = USER_DIM + ITEM_DIM + CAT_DIM + 2 + 2
        HID = [128, 64, 32]
        BN_EPS = 1e-05

        def _bn(x, g, b):
            return x * (g / jnp.sqrt(1.0 + BN_EPS)) + b
        x = jnp.concatenate([user_embeddings, item_emb[item_ids], cat_emb[category_ids], price_features, temporal_features], axis=-1)
        x = jax.nn.relu(_bn(x @ W1 + b1, g1, be1))
        x = jax.nn.relu(_bn(x @ W2 + b2, g2, be2))
        x = jax.nn.relu(_bn(x @ W3 + b3, g3, be3))
        deep_out = x @ W4 + b4
        wide_out = wide_emb1[wf1] + wide_emb2[wf2]
        flat_idx = wf1 * DIM2 + wf2
        wide_out = wide_out + cross_W[flat_idx][:, None]
        return wide_out + deep_out
    y = _L0_rec_ref(r_user_embeddings, r_price_features, r_temporal_features, L0_rec_item_emb, L0_rec_cat_emb, L0_rec_wide_emb1, L0_rec_wide_emb2, L0_rec_cross_W, L0_rec_W1, L0_rec_b1, L0_rec_W2, L0_rec_b2, L0_rec_W3, L0_rec_b3, L0_rec_W4, L0_rec_b4, L0_rec_g1, L0_rec_be1, L0_rec_g2, L0_rec_be2, L0_rec_g3, L0_rec_be3, r_item_ids, r_category_ids, r_wf1, r_wf2)
    return y

_drawn_inputs = setup_inputs


def setup_inputs(seed=0):
    import zlib

    import numpy as np

    out = dict(_drawn_inputs(seed))
    spreads = {'L0_rec_b1': (0.0, 0.1),
     'L0_rec_b2': (0.0, 0.1),
     'L0_rec_b3': (0.0, 0.1),
     'L0_rec_g1': (1.0, 0.2),
     'L0_rec_be1': (0.0, 0.1),
     'L0_rec_g2': (1.0, 0.2),
     'L0_rec_be2': (0.0, 0.1),
     'L0_rec_g3': (1.0, 0.2),
     'L0_rec_be3': (0.0, 0.1)}
    factors = {'L0_rec_item_emb': 3.53, 'L0_rec_cat_emb': 4.365, 'L0_rec_cross_W': 8.0}
    for name, (base, spread) in spreads.items():
        noise = np.random.default_rng([zlib.crc32(name.encode()), seed]).standard_normal(out[name].shape)
        drawn = base * np.exp(spread * noise) if base else spread * noise
        out[name] = jnp.asarray(drawn.astype(out[name].dtype))
    for name, factor in factors.items():
        out[name] = (out[name] * factor).astype(out[name].dtype)
    return out
```

```python
from contextlib import ExitStack

import concourse.bass as bass
from concourse import mybir

P = 128
B = 2048
TILES = B // P
GROUP = 4
GROUPS = TILES // GROUP
COLS = GROUP * P

USER, ITEM, CAT, DENSE = 64, 64, 32, 4
NUM_ITEMS, NUM_CATS, DIM = 125000, 1001, 1250
H1, H2, H3 = 128, 64, 32
BN_EPS = 1e-05
BN_SCALE = float((1.0 + BN_EPS) ** -0.5)

CHUNKS = 2
CAT_SLOTS = 4
CAT_SHIFT, CAT_MASK = 8, 255
WQ = 64
WIDE_SHIFT, WIDE_MASK = 6, 63
WIDE_SLOTS = -(-DIM // WQ)
SLAB = CAT_SLOTS * CAT

ROWS = ITEM + CAT
DIRECT = USER + DENSE

ID_ITEM, ID_WIDE, ID_CAT = 0, TILES, 3 * TILES
NIDS = 4 * TILES

T_CAT = 0
T_WIDE = T_CAT + CHUNKS * SLAB
T_QCAT = T_WIDE + 2 * WIDE_SLOTS
T_QWIDE = T_QCAT + CHUNKS
T_SLOT = T_QWIDE + 1
T_COLS = T_SLOT + WIDE_SLOTS

W_DIRECT = 0
W_ROWS = W_DIRECT + H1
W_2 = W_ROWS + H1
W_3 = W_2 + H2
W_4 = W_3 + H3
W_G = W_4 + 1
W_B = W_G + 3
W_BE = W_B + 3
W_B4 = W_BE + 3
W_COLS = W_B4 + 1

F32 = mybir.dt.float32
BF16 = mybir.dt.bfloat16
I32 = mybir.dt.int32
ALU = mybir.AluOpType
ACT = mybir.ActivationFunctionType
AX_X = mybir.AxisListType.X


def wide_deep(nc, ids, tables, weights, user_t, dense_t, item_emb, cross_w, out):
    ctx = ExitStack()
    with ctx:
        def sb(name, shape, dt):
            return ctx.enter_context(nc.sbuf_tensor(name, shape, dt))

        def pb(name):
            return ctx.enter_context(nc.psum_tensor(name, [P, COLS], F32))

        def sem(name):
            return ctx.enter_context(nc.semaphore(name))

        ids_sb = sb("ids_sb", [P, NIDS], I32)
        tab = sb("tab", [P, T_COLS], F32)
        wts = sb("wts", [P, W_COLS], F32)
        direct_t = sb("direct_t", [DIRECT, B], F32)
        ident = sb("ident", [P, P], F32)
        ident_bf = sb("ident_bf", [3 * TILES, 3 * TILES], BF16)
        dim_const = sb("dim_const", [P, TILES], I32)
        flat = sb("flat", [P, 2, TILES], I32)
        lift = sb("lift", [P, NIDS + TILES], I32)
        cap = sb("cap", [P, NIDS + TILES], I32)
        idx = sb("idx", [P, NIDS + TILES], I32)
        qi = sb("qi", [P, 3 * TILES], I32)
        qf = sb("qf", [P, 3 * TILES], F32)
        ri = sb("ri", [P, 3 * TILES], I32)
        cat_mask = sb("cat_mask", [P, TILES, CAT_SLOTS], F32)
        wide_mask = sb("wide_mask", [P, TILES, 2, WIDE_SLOTS], F32)
        q_t = sb("q_t", [3 * TILES, P], BF16)
        cat_hot = sb("cat_hot", [P, CHUNKS, B], F32)
        wide_hot = sb("wide_hot", [P, B], F32)
        cat_prod = sb("cat_prod", [P, 2, GROUP, CAT_SLOTS, CAT], F32)
        wide_prod = sb("wide_prod", [P, TILES, 2 * WIDE_SLOTS], F32)
        wide_sum = sb("wide_sum", [P, TILES], F32)
        x_rows = sb("x_rows", [P, TILES, ROWS], F32)
        rows_t = sb("rows_t", [ROWS, B], F32)
        act1 = sb("act1", [H1, B], F32)
        act2 = sb("act2", [H2, B], F32)
        act3 = sb("act3", [H3, B], F32)
        bn_s = sb("bn_s", [P, 3], F32)
        bn_bs = sb("bn_bs", [P, 3], F32)
        bn_t = sb("bn_t", [P, 3], F32)
        cross = sb("cross", [P, TILES], F32)
        base = sb("base", [P, TILES], F32)
        result = sb("result", [P, TILES], F32)

        ps_q = [pb("ps_q0"), pb("ps_q1")]
        ps_pick = [pb("ps_pick0"), pb("ps_pick1")]
        ps_x, ps_1, ps_2, ps_3 = pb("ps_x"), pb("ps_1"), pb("ps_2"), pb("ps_3")
        ps_deep = ps_q[0]

        ids_in, tab_in, wts_in = sem("ids_in"), sem("tab_in"), sem("wts_in")
        user_in, dense_in = sem("user_in"), sem("dense_in")
        ident_zero, ident_done, ident_bf_done = sem("ident_zero"), sem("ident_done"), sem("ident_bf_done")
        dim_done, mul_done, flat_done = sem("dim_done"), sem("mul_done"), sem("flat_done")
        item_capped, item_ready = sem("item_capped"), sem("item_ready")
        small_capped, small_ready = sem("small_capped"), sem("small_ready")
        cross_capped, cross_ready = sem("cross_capped"), sem("cross_ready")
        q_bits, q_float, r_bits, masks_done = sem("q_bits"), sem("q_float"), sem("r_bits"), sem("masks_done")
        q_flipped, q_t_ready = sem("q_flipped"), sem("q_t_ready")
        spread_done, hot_done = sem("spread_done"), sem("hot_done")
        picked, cat_multiplied, cat_summed = sem("picked"), sem("cat_multiplied"), sem("cat_summed")
        wide_picked, wide_multiplied, wide_done = sem("wide_picked"), sem("wide_multiplied"), sem("wide_done")
        bn_s_done, bn_bs_done, bn_done = sem("bn_s_done"), sem("bn_bs_done"), sem("bn_done")
        item_in = [sem(f"item_in{g}") for g in range(GROUPS)]
        cross_in = sem("cross_in")
        rows_flipped, rows_t_done = sem("rows_flipped"), sem("rows_t_done")
        lin1_done, lin2_done, lin3_done = sem("lin1_done"), sem("lin2_done"), sem("lin3_done")
        act1_done, act2_done, act3_done = sem("act1_done"), sem("act2_done"), sem("act3_done")
        deep_done, base_done, result_done, out_done = (
            sem("deep_done"), sem("base_done"), sem("result_done"), sem("out_done"))

        def cols(g):
            return slice(g * COLS, (g + 1) * COLS)

        def tile_cols(t):
            return slice(t * P, (t + 1) * P)

        block = ctx.enter_context(nc.Block())

        @block.sync
        def _(sp):
            sp.dma_start(ids_sb[:, :], ids).then_inc(ids_in, 16)
            sp.dma_start(direct_t[0:USER, :], user_t).then_inc(user_in, 16)
            sp.dma_start(direct_t[USER:DIRECT, :], dense_t).then_inc(dense_in, 16)
            sp.wait_ge(result_done, 1)
            sp.dma_start(out, result[:, :]).then_inc(out_done, 16)
            sp.wait_ge(out_done, 16)

        @block.gpsimd
        def _(pool):
            pool.memset(dim_const[:, :], DIM).then_inc(dim_done, 1)
            pool.memset(ident[:, :], 0.0).then_inc(ident_zero, 1)
            pool.wait_ge(ident_zero, 1)
            pool.affine_select(out=ident[:, :], in_=ident[:, :], compare_op=ALU.not_equal, fill=1.0,
                               base=0, pattern=[[-1, P]], channel_multiplier=1).then_inc(ident_done, 1)
            pool.wait_ge(ids_in, 16)
            pool.wait_ge(dim_done, 1)
            pool.tensor_tensor(flat[:, 0, :], ids_sb[:, ID_WIDE:ID_WIDE + TILES], dim_const[:, :],
                               ALU.mult).then_inc(mul_done, 1)
            pool.wait_ge(mul_done, 1)
            pool.tensor_tensor(flat[:, 1, :], flat[:, 0, :], ids_sb[:, ID_WIDE + TILES:ID_CAT],
                               ALU.add).then_inc(flat_done, 1)
            pool.wait_ge(item_ready, 1)
            for t in range(TILES):
                pool.indirect_dma_start(
                    x_rows[:, t, 0:ITEM], None, item_emb,
                    bass.IndirectOffsetOnAxis(ap=idx[:, ID_ITEM + t:ID_ITEM + t + 1], axis=0),
                ).then_inc(item_in[t // GROUP], 16)
            pool.wait_ge(cross_ready, 1)
            for t in range(TILES):
                pool.indirect_dma_start(
                    cross[:, t:t + 1], None, cross_w,
                    bass.IndirectOffsetOnAxis(ap=idx[:, NIDS + t:NIDS + t + 1], axis=0),
                ).then_inc(cross_in, 16)

        @block.scalar
        def _(act):
            act.dma_start(tab[:, :], tables).then_inc(tab_in, 16)
            act.dma_start(wts[:, :], weights).then_inc(wts_in, 16)
            act.wait_ge(ident_done, 1)
            act.copy(ident_bf[:, :], ident[0:3 * TILES, 0:3 * TILES]).then_inc(ident_bf_done, 1)
            act.wait_ge(q_flipped, 1)
            act.copy(q_t[:, :], ps_x[0:3 * TILES, 0:P]).then_inc(q_t_ready, 1)
            act.wait_ge(bn_done, 1)
            for g in range(GROUPS):
                act.wait_ge(rows_flipped, g + 1)
                act.copy(rows_t[:, cols(g)], ps_x[0:ROWS, :]).then_inc(rows_t_done, 1)
                for i, (lin_done, src, dst, done) in enumerate((
                        (lin1_done, ps_1[0:H1, :], act1[:, cols(g)], act1_done),
                        (lin2_done, ps_2[0:H2, :], act2[:, cols(g)], act2_done),
                        (lin3_done, ps_3[0:H3, :], act3[:, cols(g)], act3_done))):
                    n = dst.shape[0]
                    act.wait_ge(lin_done, g + 1)
                    act.activation(dst, src, ACT.Relu, bias=bn_t[0:n, i:i + 1],
                                   scale=bn_s[0:n, i:i + 1]).then_inc(done, 1)

        @block.vector
        def _(dve):
            def cap_ids(a, b, src, size, capped, count):
                dve.tensor_scalar(lift[:, a:b], src, 0.0, float(size), ALU.is_lt, ALU.mult)\
                   .then_inc(capped, 1)
                dve.tensor_scalar(cap[:, a:b], src, float(-size), float(size - 1), ALU.max, ALU.min)\
                   .then_inc(capped, 1)

            def resolve(a, b, capped, count, ready):
                dve.wait_ge(capped, count)
                dve.tensor_tensor(idx[:, a:b], cap[:, a:b], lift[:, a:b], ALU.add).then_inc(ready, 1)

            dve.wait_ge(ids_in, 16)
            cap_ids(0, TILES, ids_sb[:, 0:TILES], NUM_ITEMS, item_capped, 2)
            resolve(0, TILES, item_capped, 2, item_ready)
            cap_ids(ID_WIDE, ID_CAT, ids_sb[:, ID_WIDE:ID_CAT], DIM, small_capped, 2)
            cap_ids(ID_CAT, NIDS, ids_sb[:, ID_CAT:NIDS], NUM_CATS, small_capped, 4)
            resolve(ID_WIDE, NIDS, small_capped, 4, small_ready)

            dve.wait_ge(small_ready, 1)
            wide_idx, cat_idx = idx[:, ID_WIDE:ID_CAT], idx[:, ID_CAT:NIDS]
            dve.tensor_scalar(qi[:, 0:2 * TILES], wide_idx, WIDE_MASK, None, ALU.bitwise_and).then_inc(q_bits, 1)
            dve.tensor_scalar(qi[:, 2 * TILES:], cat_idx, CAT_MASK, None, ALU.bitwise_and).then_inc(q_bits, 1)
            dve.wait_ge(q_bits, 2)
            dve.tensor_copy(qf[:, :], qi[:, :]).then_inc(q_float, 1)
            dve.tensor_scalar(ri[:, 0:2 * TILES], wide_idx, WIDE_SHIFT, None,
                              ALU.logical_shift_right).then_inc(r_bits, 1)
            dve.tensor_scalar(ri[:, 2 * TILES:], cat_idx, CAT_SHIFT, None,
                              ALU.logical_shift_right).then_inc(r_bits, 1)
            dve.wait_ge(flat_done, 1)
            cap_ids(NIDS, NIDS + TILES, flat[:, 1, :], DIM * DIM, cross_capped, 2)
            resolve(NIDS, NIDS + TILES, cross_capped, 2, cross_ready)

            dve.wait_ge(tab_in, 16)
            dve.wait_ge(r_bits, 2)
            slot = tab[:, T_SLOT:T_SLOT + WIDE_SLOTS]
            dve.tensor_tensor(
                cat_mask[:, :, :],
                ri[:, 2 * TILES:].unsqueeze(2).to_broadcast([P, TILES, CAT_SLOTS]),
                slot[:, 0:CAT_SLOTS].unsqueeze(1).to_broadcast([P, TILES, CAT_SLOTS]),
                ALU.is_equal).then_inc(masks_done, 1)

            def cat_onehots(g):
                dve.wait_ge(spread_done, g + 1)
                for c in range(CHUNKS):
                    dve.tensor_scalar(cat_hot[:, c, cols(g)], ps_q[g % 2][:, :],
                                      tab[:, T_QCAT + c:T_QCAT + c + 1], None,
                                      ALU.is_equal).then_inc(hot_done, 1)

            def wide_onehots(g):
                dve.wait_ge(spread_done, GROUPS + g + 1)
                dve.tensor_scalar(wide_hot[:, cols(g)], ps_q[g % 2][:, :],
                                  tab[:, T_QWIDE:T_QWIDE + 1], None, ALU.is_equal).then_inc(hot_done, 1)

            def cat_slots(g):
                dve.wait_ge(picked, g + 1)
                if g == 0:
                    dve.wait_ge(masks_done, 1)
                if g >= 2:
                    dve.wait_ge(cat_summed, g - 1)
                mask = cat_mask[:, g * GROUP:(g + 1) * GROUP, :].rearrange("p t r -> p (t r)")
                dve.tensor_tensor(
                    cat_prod[:, g % 2].rearrange("p t r d -> p (t r) d"),
                    ps_pick[g % 2][:, :].rearrange("p (tr d) -> p tr d", d=CAT),
                    mask.unsqueeze(2).to_broadcast([P, GROUP * CAT_SLOTS, CAT]),
                    ALU.mult).then_inc(cat_multiplied, 1)
                dve.wait_ge(cat_multiplied, g + 1)
                dve.tensor_reduce(x_rows[:, g * GROUP:(g + 1) * GROUP, ITEM:ROWS],
                                  cat_prod[:, g % 2].rearrange("p t r d -> p t d r"),
                                  AX_X, ALU.add).then_inc(cat_summed, 1)

            cat_onehots(0)
            cat_onehots(1)
            dve.wait_ge(wts_in, 16)
            dve.tensor_scalar(bn_s[:, :], wts[:, W_G:W_G + 3], BN_SCALE, None, ALU.mult).then_inc(bn_s_done, 1)
            dve.wait_ge(bn_s_done, 1)
            dve.tensor_tensor(bn_bs[:, :], wts[:, W_B:W_B + 3], bn_s[:, :], ALU.mult).then_inc(bn_bs_done, 1)
            dve.wait_ge(bn_bs_done, 1)
            dve.tensor_tensor(bn_t[:, :], bn_bs[:, :], wts[:, W_BE:W_BE + 3], ALU.add).then_inc(bn_done, 1)
            cat_slots(0)
            cat_onehots(2)
            cat_slots(1)
            cat_onehots(3)
            cat_slots(2)
            wide_onehots(0)
            cat_slots(3)
            wide_onehots(1)
            for w in range(2):
                dve.tensor_tensor(
                    wide_mask[:, :, w, :],
                    ri[:, w * TILES:(w + 1) * TILES].unsqueeze(2).to_broadcast([P, TILES, WIDE_SLOTS]),
                    slot.unsqueeze(1).to_broadcast([P, TILES, WIDE_SLOTS]),
                    ALU.is_equal).then_inc(masks_done, 1)
            wide_onehots(2)
            wide_onehots(3)
            dve.wait_ge(masks_done, 3)
            half = TILES // 2
            for h in range(2):
                dve.wait_ge(wide_picked, h + 1)
                dve.tensor_tensor(
                    wide_prod[:, h * half:(h + 1) * half, :],
                    ps_pick[h][:, 0:half * 2 * WIDE_SLOTS].rearrange("p (t r) -> p t r", t=half),
                    wide_mask[:, h * half:(h + 1) * half].rearrange("p t w r -> p t (w r)"),
                    ALU.mult).then_inc(wide_multiplied, 1)
            dve.wait_ge(wide_multiplied, 2)
            dve.tensor_reduce(wide_sum[:, :], wide_prod[:, :, :], AX_X, ALU.add).then_inc(wide_done, 1)
            dve.wait_ge(deep_done, 1)
            dve.wait_ge(wide_done, 1)
            dve.scalar_tensor_tensor(base[:, :], ps_deep[:, 0:TILES], wts[:, W_B4:W_B4 + 1], wide_sum[:, :],
                                     ALU.add, ALU.add).then_inc(base_done, 1)
            dve.wait_ge(base_done, 1)
            dve.wait_ge(cross_in, 16 * TILES)
            dve.tensor_tensor(result[:, :], base[:, :], cross[:, :], ALU.add).then_inc(result_done, 1)

        @block.tensor
        def _(pe):
            def spread(g, wide):
                n = (GROUPS if wide else 0) + g
                if n >= 2:
                    pe.wait_ge(hot_done, CHUNKS * (n - 1) if n - 1 <= GROUPS
                               else CHUNKS * GROUPS + n - 1 - GROUPS)
                for j in range(GROUP):
                    t = g * GROUP + j
                    if wide:
                        for w in range(2):
                            pick = ident_bf[0:2 * TILES, w * TILES + t:w * TILES + t + 1]
                            last = pe.matmul(ps_q[g % 2][w * WQ:(w + 1) * WQ, tile_cols(j)],
                                             pick.to_broadcast([2 * TILES, WQ]), q_t[0:2 * TILES, :],
                                             start=True, stop=True)
                    else:
                        a, b = 2 * TILES, 3 * TILES
                        pick = ident_bf[a:b, a + t:a + t + 1]
                        last = pe.matmul(ps_q[g % 2][:, tile_cols(j)], pick.to_broadcast([TILES, P]),
                                         q_t[a:b, :], start=True, stop=True)
                last.then_inc(spread_done, 1)

            def pick_cat(g):
                pe.wait_ge(hot_done, CHUNKS * (g + 1))
                if g >= 2:
                    pe.wait_ge(cat_multiplied, g - 1)
                for j in range(GROUP):
                    for c in range(CHUNKS):
                        last = pe.matmul(ps_pick[g % 2][:, tile_cols(j)],
                                         cat_hot[:, c, tile_cols(g * GROUP + j)],
                                         tab[:, T_CAT + c * SLAB:T_CAT + (c + 1) * SLAB],
                                         start=(c == 0), stop=(c == CHUNKS - 1))
                last.then_inc(picked, 1)

            def pick_wide(h):
                half = TILES // 2
                w = 2 * WIDE_SLOTS
                pe.wait_ge(hot_done, CHUNKS * GROUPS + GROUPS // 2 * (h + 1))
                pe.wait_ge(cat_multiplied, GROUPS - 1 + h)
                for j in range(half):
                    last = pe.matmul(ps_pick[h][:, j * w:(j + 1) * w], wide_hot[:, tile_cols(h * half + j)],
                                     tab[:, T_WIDE:T_WIDE + w], start=True, stop=True)
                last.then_inc(wide_picked, 1)

            def flip_rows(g):
                pe.wait_ge(item_in[g], 16 * GROUP)
                pe.wait_ge(cat_summed, g + 1)
                if g >= 1:
                    pe.wait_ge(rows_t_done, g)
                for j in range(GROUP):
                    last = pe.transpose(ps_x[0:ROWS, tile_cols(j)], x_rows[:, g * GROUP + j, :], ident[:, :])
                last.then_inc(rows_flipped, 1)

            def layer1_direct(g):
                if g >= 1:
                    pe.wait_ge(act1_done, g)
                pe.matmul(ps_1[:, :], wts[0:DIRECT, W_DIRECT:W_DIRECT + H1], direct_t[:, cols(g)],
                          start=True, stop=False)

            def layer1_rows(g):
                pe.wait_ge(rows_t_done, g + 1)
                pe.matmul(ps_1[:, :], wts[0:ROWS, W_ROWS:W_ROWS + H1], rows_t[:, cols(g)],
                          start=False, stop=True).then_inc(lin1_done, 1)

            def layer2(g):
                pe.wait_ge(act1_done, g + 1)
                if g >= 1:
                    pe.wait_ge(act2_done, g)
                pe.matmul(ps_2[0:H2, :], wts[0:H1, W_2:W_2 + H2], act1[:, cols(g)],
                          start=True, stop=True).then_inc(lin2_done, 1)

            def layer3(g):
                pe.wait_ge(act2_done, g + 1)
                if g >= 1:
                    pe.wait_ge(act3_done, g)
                pe.matmul(ps_3[0:H3, :], wts[0:H2, W_3:W_3 + H3], act2[:, cols(g)],
                          start=True, stop=True).then_inc(lin3_done, 1)

            def layer4(g):
                pe.wait_ge(act3_done, g + 1)
                for j in range(GROUP):
                    t = g * GROUP + j
                    last = pe.matmul(ps_deep[:, t:t + 1], act3[:, tile_cols(t)], wts[0:H3, W_4:W_4 + 1],
                                     start=True, stop=True)
                if g == GROUPS - 1:
                    last.then_inc(deep_done, 1)

            pe.wait_ge(ident_done, 1)
            pe.wait_ge(q_float, 1)
            pe.transpose(ps_x[0:3 * TILES, 0:P], qf[:, :], ident[:, :]).then_inc(q_flipped, 1)
            pe.wait_ge(ident_bf_done, 1)
            pe.wait_ge(q_t_ready, 1)
            spread(0, False)
            spread(1, False)
            pe.wait_ge(tab_in, 16)
            pick_cat(0)
            spread(2, False)
            pick_cat(1)
            spread(3, False)
            pick_cat(2)
            spread(0, True)
            pick_cat(3)
            spread(1, True)
            pe.wait_ge(wts_in, 16)
            pe.wait_ge(user_in, 16)
            pe.wait_ge(dense_in, 16)
            layer1_direct(0)
            flip_rows(0)
            spread(2, True)
            layer1_rows(0)
            spread(3, True)
            layer2(0)
            pick_wide(0)
            layer3(0)
            pick_wide(1)
            for g in range(1, GROUPS):
                layer1_direct(g)
                flip_rows(g)
                layer4(g - 1)
                layer1_rows(g)
                layer2(g)
                layer3(g)
            layer4(GROUPS - 1)


def kernel(**inputs):
    import numpy as np
    import concourse.bacc as bacc
    from concourse.bass_utils import run_bass_kernel_spmd

    a = {k: np.asarray(v) for k, v in inputs.items()}
    f32 = np.float32

    ids = np.concatenate([a[k].reshape(P, TILES) for k in
                          ("r_item_ids", "r_wf1", "r_wf2", "r_category_ids")], axis=1)

    tables = np.zeros((P, T_COLS), f32)
    cat = np.zeros((CAT_SLOTS * CHUNKS * P, CAT), f32)
    cat[:NUM_CATS] = a["L0_rec_cat_emb"]
    tables[:, T_CAT:T_WIDE] = cat.reshape(CAT_SLOTS, CHUNKS, P, CAT).transpose(2, 1, 0, 3).reshape(P, -1)
    for w, name in enumerate(("L0_rec_wide_emb1", "L0_rec_wide_emb2")):
        wide = np.zeros(WIDE_SLOTS * WQ, f32)
        wide[:DIM] = a[name][:, 0]
        tables[w * WQ:(w + 1) * WQ, T_WIDE + w * WIDE_SLOTS:T_WIDE + (w + 1) * WIDE_SLOTS] = \
            wide.reshape(WIDE_SLOTS, WQ).T
    part = np.arange(P)
    for c in range(CHUNKS):
        tables[:, T_QCAT + c] = part + c * P
    tables[:, T_QWIDE] = part % WQ
    tables[:, T_SLOT:T_SLOT + WIDE_SLOTS] = np.arange(WIDE_SLOTS)

    weights = np.zeros((P, W_COLS), f32)
    w1 = a["L0_rec_W1"]
    weights[:USER, W_DIRECT:W_DIRECT + H1] = w1[:USER]
    weights[USER:DIRECT, W_DIRECT:W_DIRECT + H1] = w1[USER + ROWS:]
    weights[:ROWS, W_ROWS:W_ROWS + H1] = w1[USER:USER + ROWS]
    weights[:H1, W_2:W_2 + H2] = a["L0_rec_W2"]
    weights[:H2, W_3:W_3 + H3] = a["L0_rec_W3"]
    weights[:H3, W_4:W_4 + 1] = a["L0_rec_W4"]
    for i, n in enumerate((H1, H2, H3)):
        weights[:n, W_G + i] = a[f"L0_rec_g{i + 1}"]
        weights[:n, W_B + i] = a[f"L0_rec_b{i + 1}"]
        weights[:n, W_BE + i] = a[f"L0_rec_be{i + 1}"]
    weights[:, W_B4] = a["L0_rec_b4"]

    def flip(x):
        return np.ascontiguousarray(x.reshape(P, TILES, -1).transpose(2, 1, 0).reshape(-1, B))

    arrays = {
        "ids": np.ascontiguousarray(ids),
        "tables": tables,
        "weights": weights,
        "user_t": flip(a["r_user_embeddings"]),
        "dense_t": flip(np.concatenate([a["r_price_features"], a["r_temporal_features"]], axis=1)),
        "item_emb": np.ascontiguousarray(a["L0_rec_item_emb"]),
        "cross_w": np.ascontiguousarray(a["L0_rec_cross_W"]).reshape(-1, 1),
    }
    nc = bacc.Bacc("TRN2", target_bir_lowering=False, num_devices=1)
    args = [nc.dram_tensor(k, v.shape, mybir.dt.from_np(v.dtype), kind="ExternalInput").ap()
            for k, v in arrays.items()]
    out = nc.dram_tensor("out", (P, TILES), F32, kind="ExternalOutput").ap()
    wide_deep(nc, *args, out)
    r = run_bass_kernel_spmd(nc, [arrays], core_ids=[0])
    return r.results[0]["out"].reshape(B, 1)
```

```python
from contextlib import ExitStack

import concourse.bass as bass
from concourse import mybir

P = 128
B = 2048
TILES = B // P
GROUP = 4
GROUPS = TILES // GROUP
COLS = GROUP * P

USER, ITEM, CAT, DENSE = 64, 64, 32, 4
NUM_ITEMS, NUM_CATS, DIM = 125000, 1001, 1250
H1, H2, H3 = 128, 64, 32
PAIRS = GROUPS // 2
BN_EPS = 1e-05
BN_SCALE = float((1.0 + BN_EPS) ** -0.5)

CHUNKS = 2
CAT_SLOTS = 4
CAT_SHIFT, CAT_MASK = 8, 255
WQ = 64
WIDE_SHIFT, WIDE_MASK = 6, 63
WIDE_SLOTS = -(-DIM // WQ)
SLAB = CAT_SLOTS * CAT

ROWS = ITEM + CAT
DIRECT = USER + DENSE

ID_ITEM, ID_WIDE, ID_CAT = 0, TILES, 3 * TILES
NIDS = 4 * TILES

T_CAT = 0
T_WIDE = T_CAT + CHUNKS * SLAB
T_QCAT = T_WIDE + 2 * WIDE_SLOTS
T_QWIDE = T_QCAT + CHUNKS
T_SLOT = T_QWIDE + 1
T_COLS = T_SLOT + WIDE_SLOTS

W_DIRECT = 0
W_ROWS = W_DIRECT + H1
W_2 = W_ROWS + H1
W_3 = W_2 + H2
W_4 = W_3 + 2 * H3
W_G = W_4 + GROUPS
W_B = W_G + 3
W_BE = W_B + 3
W_B4 = W_BE + 3
W_COLS = W_B4 + 1

F32 = mybir.dt.float32
BF16 = mybir.dt.bfloat16
I32 = mybir.dt.int32
ALU = mybir.AluOpType
ACT = mybir.ActivationFunctionType
AX_X = mybir.AxisListType.X


def wide_deep(nc, ids, tables, weights, user_t, dense_t, item_emb, cross_w, out):
    ctx = ExitStack()
    with ctx:
        def sb(name, shape, dt):
            return ctx.enter_context(nc.sbuf_tensor(name, shape, dt))

        def pb(name):
            return ctx.enter_context(nc.psum_tensor(name, [P, COLS], F32))

        def sem(name):
            return ctx.enter_context(nc.semaphore(name))

        ids_sb = sb("ids_sb", [P, NIDS], I32)
        tab = sb("tab", [P, T_COLS], F32)
        wts = sb("wts", [P, W_COLS], F32)
        direct_t = sb("direct_t", [DIRECT, B], F32)
        ident = sb("ident", [P, P], F32)
        ident_bf = sb("ident_bf", [3 * TILES, 3 * TILES], BF16)
        dim_const = sb("dim_const", [P, TILES], I32)
        flat = sb("flat", [P, 2, TILES], I32)
        lift = sb("lift", [P, NIDS + TILES], I32)
        cap = sb("cap", [P, NIDS + TILES], I32)
        idx = sb("idx", [P, NIDS + TILES], I32)
        qi = sb("qi", [P, 3 * TILES], I32)
        qf = sb("qf", [P, 3 * TILES], F32)
        ri = sb("ri", [P, 3 * TILES], I32)
        cat_mask = sb("cat_mask", [P, TILES, CAT_SLOTS], F32)
        wide_mask = sb("wide_mask", [P, TILES, 2, WIDE_SLOTS], F32)
        q_t = sb("q_t", [3 * TILES, P], BF16)
        cat_hot = sb("cat_hot", [P, CHUNKS, B], F32)
        wide_hot = sb("wide_hot", [P, B], F32)
        cat_prod = sb("cat_prod", [P, 2, GROUP, CAT_SLOTS, CAT], F32)
        wide_prod = sb("wide_prod", [P, TILES, 2 * WIDE_SLOTS], F32)
        wide_sum = sb("wide_sum", [P, TILES], F32)
        x_rows = sb("x_rows", [P, TILES, ROWS], F32)
        rows_t = sb("rows_t", [ROWS, B], F32)
        act1 = sb("act1", [H1, B], F32)
        act2 = sb("act2", [2 * H2, PAIRS, COLS], F32)
        act3 = sb("act3", [GROUPS * H3, COLS], F32)
        bn_s = sb("bn_s", [P, 3], F32)
        bn_bs = sb("bn_bs", [P, 3], F32)
        bn_t = sb("bn_t", [P, 3], F32)
        cross = sb("cross", [P, TILES], F32)
        base = sb("base", [P, TILES], F32)
        result = sb("result", [P, TILES], F32)

        ps_q = [pb("ps_q0"), pb("ps_q1")]
        ps_pick = [pb("ps_pick0"), pb("ps_pick1")]
        ps_x, ps_1, ps_2, ps_3 = pb("ps_x"), pb("ps_1"), pb("ps_2"), pb("ps_3")
        ps_deep = ps_q[0]

        ids_in, tab_in, wts_in = sem("ids_in"), sem("tab_in"), sem("wts_in")
        user_in, dense_in = sem("user_in"), sem("dense_in")
        ident_zero, ident_done, ident_bf_done = sem("ident_zero"), sem("ident_done"), sem("ident_bf_done")
        dim_done, mul_done, flat_done = sem("dim_done"), sem("mul_done"), sem("flat_done")
        item_capped, item_ready = sem("item_capped"), sem("item_ready")
        small_capped, small_ready = sem("small_capped"), sem("small_ready")
        cross_capped, cross_ready = sem("cross_capped"), sem("cross_ready")
        q_bits, q_float, r_bits, masks_done = sem("q_bits"), sem("q_float"), sem("r_bits"), sem("masks_done")
        q_flipped, q_t_ready = sem("q_flipped"), sem("q_t_ready")
        spread_done, hot_done = sem("spread_done"), sem("hot_done")
        picked, cat_multiplied, cat_summed = sem("picked"), sem("cat_multiplied"), sem("cat_summed")
        wide_picked, wide_multiplied, wide_done = sem("wide_picked"), sem("wide_multiplied"), sem("wide_done")
        bn_s_done, bn_bs_done, bn_done = sem("bn_s_done"), sem("bn_bs_done"), sem("bn_done")
        item_in = [sem(f"item_in{g}") for g in range(GROUPS)]
        cross_in = sem("cross_in")
        rows_flipped, rows_t_done = sem("rows_flipped"), sem("rows_t_done")
        lin1_done, lin2_done, lin3_done = sem("lin1_done"), sem("lin2_done"), sem("lin3_done")
        act1_done, act2_done, act3_done = sem("act1_done"), sem("act2_done"), sem("act3_done")
        deep_done, base_done, result_done, out_done = (
            sem("deep_done"), sem("base_done"), sem("result_done"), sem("out_done"))

        def cols(g):
            return slice(g * COLS, (g + 1) * COLS)

        def tile_cols(t):
            return slice(t * P, (t + 1) * P)

        block = ctx.enter_context(nc.Block())

        @block.sync
        def _(sp):
            sp.dma_start(ids_sb[:, :], ids).then_inc(ids_in, 16)
            sp.dma_start(direct_t[0:USER, :], user_t).then_inc(user_in, 16)
            sp.dma_start(direct_t[USER:DIRECT, :], dense_t).then_inc(dense_in, 16)
            sp.wait_ge(result_done, 1)
            sp.dma_start(out, result[:, :]).then_inc(out_done, 16)
            sp.wait_ge(out_done, 16)

        @block.gpsimd
        def _(pool):
            pool.memset(dim_const[:, :], DIM).then_inc(dim_done, 1)
            pool.memset(ident[:, :], 0.0).then_inc(ident_zero, 1)
            pool.wait_ge(ident_zero, 1)
            pool.affine_select(out=ident[:, :], in_=ident[:, :], compare_op=ALU.not_equal, fill=1.0,
                               base=0, pattern=[[-1, P]], channel_multiplier=1).then_inc(ident_done, 1)
            pool.wait_ge(ids_in, 16)
            pool.wait_ge(dim_done, 1)
            pool.tensor_tensor(flat[:, 0, :], ids_sb[:, ID_WIDE:ID_WIDE + TILES], dim_const[:, :],
                               ALU.mult).then_inc(mul_done, 1)
            pool.wait_ge(mul_done, 1)
            pool.tensor_tensor(flat[:, 1, :], flat[:, 0, :], ids_sb[:, ID_WIDE + TILES:ID_CAT],
                               ALU.add).then_inc(flat_done, 1)
            pool.wait_ge(item_ready, 1)
            for t in range(TILES):
                pool.indirect_dma_start(
                    x_rows[:, t, 0:ITEM], None, item_emb,
                    bass.IndirectOffsetOnAxis(ap=idx[:, ID_ITEM + t:ID_ITEM + t + 1], axis=0),
                ).then_inc(item_in[t // GROUP], 16)
            pool.wait_ge(cross_ready, 1)
            for t in range(TILES):
                pool.indirect_dma_start(
                    cross[:, t:t + 1], None, cross_w,
                    bass.IndirectOffsetOnAxis(ap=idx[:, NIDS + t:NIDS + t + 1], axis=0),
                ).then_inc(cross_in, 16)

        @block.scalar
        def _(act):
            act.dma_start(tab[:, :], tables).then_inc(tab_in, 16)
            act.dma_start(wts[:, :], weights).then_inc(wts_in, 16)
            act.wait_ge(ident_done, 1)
            act.copy(ident_bf[:, :], ident[0:3 * TILES, 0:3 * TILES]).then_inc(ident_bf_done, 1)
            act.wait_ge(q_flipped, 1)
            act.copy(q_t[:, :], ps_x[0:3 * TILES, 0:P]).then_inc(q_t_ready, 1)
            act.wait_ge(bn_done, 1)
            def relu(dst, src, layer):
                return act.activation(dst, src, ACT.Relu, bias=bn_t[:, layer:layer + 1],
                                      scale=bn_s[:, layer:layer + 1])

            for g in range(GROUPS):
                act.wait_ge(rows_flipped, g + 1)
                act.copy(rows_t[:, cols(g)], ps_x[0:ROWS, :]).then_inc(rows_t_done, 1)
                act.wait_ge(lin1_done, g + 1)
                relu(act1[:, cols(g)], ps_1[:, :], 0).then_inc(act1_done, 1)
                if g % 2:
                    act.wait_ge(lin2_done, g + 1)
                    relu(act2[:, g // 2, :], ps_2[:, :], 1).then_inc(act2_done, 1)
            act.wait_ge(lin3_done, PAIRS)
            relu(act3[:, :], ps_3[:, :], 2).then_inc(act3_done, 1)

        @block.vector
        def _(dve):
            def cap_ids(a, b, src, size, capped):
                dve.tensor_scalar(lift[:, a:b], src, 0.0, float(size), ALU.is_lt, ALU.mult)\
                   .then_inc(capped, 1)
                dve.tensor_scalar(cap[:, a:b], src, float(-size), float(size - 1), ALU.max, ALU.min)\
                   .then_inc(capped, 1)

            def resolve(a, b, capped, count, ready):
                dve.wait_ge(capped, count)
                dve.scalar_tensor_tensor(idx[:, a:b], cap[:, a:b], float(-DIM * DIM), lift[:, a:b],
                                         ALU.max, ALU.add).then_inc(ready, 1)

            dve.wait_ge(ids_in, 16)
            cap_ids(0, TILES, ids_sb[:, 0:TILES], NUM_ITEMS, item_capped)
            resolve(0, TILES, item_capped, 2, item_ready)
            cap_ids(ID_WIDE, ID_CAT, ids_sb[:, ID_WIDE:ID_CAT], DIM, small_capped)
            cap_ids(ID_CAT, NIDS, ids_sb[:, ID_CAT:NIDS], NUM_CATS, small_capped)
            resolve(ID_WIDE, NIDS, small_capped, 4, small_ready)

            dve.wait_ge(small_ready, 1)
            wide_idx, cat_idx = idx[:, ID_WIDE:ID_CAT], idx[:, ID_CAT:NIDS]
            dve.tensor_scalar(qi[:, 0:2 * TILES], wide_idx, WIDE_MASK, None, ALU.bitwise_and).then_inc(q_bits, 1)
            dve.tensor_scalar(qi[:, 2 * TILES:], cat_idx, CAT_MASK, None, ALU.bitwise_and).then_inc(q_bits, 1)
            dve.wait_ge(q_bits, 2)
            dve.tensor_copy(qf[:, :], qi[:, :]).then_inc(q_float, 1)
            dve.tensor_scalar(ri[:, 0:2 * TILES], wide_idx, WIDE_SHIFT, None,
                              ALU.logical_shift_right).then_inc(r_bits, 1)
            dve.tensor_scalar(ri[:, 2 * TILES:], cat_idx, CAT_SHIFT, None,
                              ALU.logical_shift_right).then_inc(r_bits, 1)
            dve.wait_ge(flat_done, 1)
            cap_ids(NIDS, NIDS + TILES, flat[:, 1, :], DIM * DIM, cross_capped)
            resolve(NIDS, NIDS + TILES, cross_capped, 2, cross_ready)

            dve.wait_ge(tab_in, 16)
            dve.wait_ge(r_bits, 2)
            slot = tab[:, T_SLOT:T_SLOT + WIDE_SLOTS]
            dve.tensor_tensor(
                cat_mask[:, :, :],
                ri[:, 2 * TILES:].unsqueeze(2).to_broadcast([P, TILES, CAT_SLOTS]),
                slot[:, 0:CAT_SLOTS].unsqueeze(1).to_broadcast([P, TILES, CAT_SLOTS]),
                ALU.is_equal).then_inc(masks_done, 1)

            def cat_onehots(g):
                dve.wait_ge(spread_done, g + 1)
                for c in range(CHUNKS):
                    dve.tensor_scalar(cat_hot[:, c, cols(g)], ps_q[g % 2][:, :],
                                      tab[:, T_QCAT + c:T_QCAT + c + 1], None,
                                      ALU.is_equal).then_inc(hot_done, 1)

            def wide_onehots(g):
                dve.wait_ge(spread_done, GROUPS + g + 1)
                dve.tensor_scalar(wide_hot[:, cols(g)], ps_q[g % 2][:, :],
                                  tab[:, T_QWIDE:T_QWIDE + 1], None, ALU.is_equal).then_inc(hot_done, 1)

            def cat_slots(g):
                dve.wait_ge(picked, g + 1)
                if g == 0:
                    dve.wait_ge(masks_done, 1)
                if g >= 2:
                    dve.wait_ge(cat_summed, g - 1)
                mask = cat_mask[:, g * GROUP:(g + 1) * GROUP, :].rearrange("p t r -> p (t r)")
                dve.tensor_tensor(
                    cat_prod[:, g % 2].rearrange("p t r d -> p (t r) d"),
                    ps_pick[g % 2][:, :].rearrange("p (tr d) -> p tr d", d=CAT),
                    mask.unsqueeze(2).to_broadcast([P, GROUP * CAT_SLOTS, CAT]),
                    ALU.mult).then_inc(cat_multiplied, 1)
                dve.wait_ge(cat_multiplied, g + 1)
                dve.tensor_reduce(x_rows[:, g * GROUP:(g + 1) * GROUP, ITEM:ROWS],
                                  cat_prod[:, g % 2].rearrange("p t r d -> p t d r"),
                                  AX_X, ALU.add).then_inc(cat_summed, 1)

            cat_onehots(0)
            cat_onehots(1)
            dve.wait_ge(wts_in, 16)
            dve.tensor_scalar(bn_s[:, :], wts[:, W_G:W_G + 3], BN_SCALE, None, ALU.mult).then_inc(bn_s_done, 1)
            dve.wait_ge(bn_s_done, 1)
            dve.tensor_tensor(bn_bs[:, :], wts[:, W_B:W_B + 3], bn_s[:, :], ALU.mult).then_inc(bn_bs_done, 1)
            dve.wait_ge(bn_bs_done, 1)
            dve.tensor_tensor(bn_t[:, :], bn_bs[:, :], wts[:, W_BE:W_BE + 3], ALU.add).then_inc(bn_done, 1)
            cat_slots(0)
            cat_onehots(2)
            cat_slots(1)
            cat_onehots(3)
            cat_slots(2)
            wide_onehots(0)
            cat_slots(3)
            wide_onehots(1)
            for w in range(2):
                dve.tensor_tensor(
                    wide_mask[:, :, w, :],
                    ri[:, w * TILES:(w + 1) * TILES].unsqueeze(2).to_broadcast([P, TILES, WIDE_SLOTS]),
                    slot.unsqueeze(1).to_broadcast([P, TILES, WIDE_SLOTS]),
                    ALU.is_equal).then_inc(masks_done, 1)
            wide_onehots(2)
            wide_onehots(3)
            dve.wait_ge(masks_done, 3)
            half = TILES // 2
            for h in range(2):
                dve.wait_ge(wide_picked, 2 * (h + 1))
                dve.tensor_tensor(
                    wide_prod[:, h * half:(h + 1) * half, :],
                    ps_pick[h][:, 0:half * 2 * WIDE_SLOTS].rearrange("p (t r) -> p t r", t=half),
                    wide_mask[:, h * half:(h + 1) * half].rearrange("p t w r -> p t (w r)"),
                    ALU.mult).then_inc(wide_multiplied, 1)
            dve.wait_ge(wide_multiplied, 2)
            dve.tensor_reduce(wide_sum[:, :], wide_prod[:, :, :], AX_X, ALU.add).then_inc(wide_done, 1)
            dve.wait_ge(deep_done, 1)
            dve.wait_ge(wide_done, 1)
            dve.scalar_tensor_tensor(base[:, :], ps_deep[:, 0:TILES], wts[:, W_B4:W_B4 + 1], wide_sum[:, :],
                                     ALU.add, ALU.add).then_inc(base_done, 1)
            dve.wait_ge(base_done, 1)
            dve.wait_ge(cross_in, 16 * TILES)
            dve.tensor_tensor(result[:, :], base[:, :], cross[:, :], ALU.add).then_inc(result_done, 1)

        @block.tensor
        def _(pe):
            def spread(g, wide):
                n = (GROUPS if wide else 0) + g
                if n >= 2:
                    pe.wait_ge(hot_done, CHUNKS * (n - 1) if n - 1 <= GROUPS
                               else CHUNKS * GROUPS + n - 1 - GROUPS)
                for j in range(GROUP):
                    t = g * GROUP + j
                    if wide:
                        for w in range(2):
                            pick = ident_bf[0:2 * TILES, w * TILES + t:w * TILES + t + 1]
                            last = pe.matmul(ps_q[g % 2][w * WQ:(w + 1) * WQ, tile_cols(j)],
                                             pick.to_broadcast([2 * TILES, WQ]), q_t[0:2 * TILES, :],
                                             start=True, stop=True)
                    else:
                        a, b = 2 * TILES, 3 * TILES
                        pick = ident_bf[a:b, a + t:a + t + 1]
                        last = pe.matmul(ps_q[g % 2][:, tile_cols(j)], pick.to_broadcast([TILES, P]),
                                         q_t[a:b, :], start=True, stop=True)
                last.then_inc(spread_done, 1)

            def pick_cat(g):
                pe.wait_ge(hot_done, CHUNKS * (g + 1))
                if g >= 2:
                    pe.wait_ge(cat_multiplied, g - 1)
                for j in range(GROUP):
                    for c in range(CHUNKS):
                        last = pe.matmul(ps_pick[g % 2][:, tile_cols(j)],
                                         cat_hot[:, c, tile_cols(g * GROUP + j)],
                                         tab[:, T_CAT + c * SLAB:T_CAT + (c + 1) * SLAB],
                                         start=(c == 0), stop=(c == CHUNKS - 1))
                last.then_inc(picked, 1)

            def pick_wide(g):
                w = 2 * WIDE_SLOTS
                pe.wait_ge(hot_done, CHUNKS * GROUPS + g + 1)
                if g % 2 == 0:
                    pe.wait_ge(cat_multiplied, GROUPS - 1 + g // 2)
                for j in range(GROUP):
                    at = (g % 2 * GROUP + j) * w
                    last = pe.matmul(ps_pick[g // 2][:, at:at + w], wide_hot[:, tile_cols(g * GROUP + j)],
                                     tab[:, T_WIDE:T_WIDE + w], start=True, stop=True)
                last.then_inc(wide_picked, 1)

            def flip_rows(g):
                pe.wait_ge(item_in[g], 16 * GROUP)
                pe.wait_ge(cat_summed, g + 1)
                if g >= 1:
                    pe.wait_ge(rows_t_done, g)
                for j in range(GROUP):
                    last = pe.transpose(ps_x[0:ROWS, tile_cols(j)], x_rows[:, g * GROUP + j, :], ident[:, :])
                last.then_inc(rows_flipped, 1)

            def layer1_direct(g):
                if g >= 1:
                    pe.wait_ge(act1_done, g)
                pe.matmul(ps_1[:, :], wts[0:DIRECT, W_DIRECT:W_DIRECT + H1], direct_t[:, cols(g)],
                          start=True, stop=False)

            def layer1_rows(g):
                pe.wait_ge(rows_t_done, g + 1)
                pe.matmul(ps_1[:, :], wts[0:ROWS, W_ROWS:W_ROWS + H1], rows_t[:, cols(g)],
                          start=False, stop=True).then_inc(lin1_done, 1)

            def layer2(g):
                pe.wait_ge(act1_done, g + 1)
                if g >= 2:
                    pe.wait_ge(act2_done, g // 2)
                h = g % 2 * H2
                pe.matmul(ps_2[h:h + H2, :], wts[0:H1, W_2:W_2 + H2], act1[:, cols(g)],
                          start=True, stop=True).then_inc(lin2_done, 1)

            def layer3(pair):
                pe.wait_ge(act2_done, pair + 1)
                h = pair * 2 * H3
                pe.matmul(ps_3[h:h + 2 * H3, :], wts[:, W_3:W_3 + 2 * H3], act2[:, pair, :],
                          start=True, stop=True).then_inc(lin3_done, 1)

            def layer4():
                pe.wait_ge(act3_done, 1)
                for j in range(GROUP):
                    last = pe.matmul(ps_deep[:, j:TILES:GROUP], act3[:, tile_cols(j)],
                                     wts[:, W_4:W_4 + GROUPS], start=True, stop=True)
                last.then_inc(deep_done, 1)

            pe.wait_ge(ident_done, 1)
            pe.wait_ge(q_float, 1)
            pe.transpose(ps_x[0:3 * TILES, 0:P], qf[:, :], ident[:, :]).then_inc(q_flipped, 1)
            pe.wait_ge(ident_bf_done, 1)
            pe.wait_ge(q_t_ready, 1)
            spread(0, False)
            spread(1, False)
            pe.wait_ge(wts_in, 16)
            pe.wait_ge(user_in, 16)
            pe.wait_ge(dense_in, 16)
            layer1_direct(0)
            pe.wait_ge(tab_in, 16)
            pick_cat(0)
            spread(2, False)
            pick_cat(1)
            spread(3, False)
            flip_rows(0)
            pick_cat(2)
            spread(0, True)
            layer1_rows(0)
            pick_cat(3)
            layer1_direct(1)
            spread(1, True)
            flip_rows(1)
            layer2(0)
            spread(2, True)
            layer1_rows(1)
            spread(3, True)
            pick_wide(0)
            layer1_direct(2)
            layer2(1)
            flip_rows(2)
            pick_wide(1)
            layer1_rows(2)
            flip_rows(3)
            pick_wide(2)
            layer1_direct(3)
            layer1_rows(3)
            layer2(2)
            pick_wide(3)
            layer2(3)
            layer3(0)
            layer3(1)
            layer4()


def kernel(**inputs):
    import numpy as np
    import concourse.bacc as bacc
    from concourse.bass_utils import run_bass_kernel_spmd

    a = {k: np.asarray(v) for k, v in inputs.items()}
    f32 = np.float32

    ids = np.concatenate([a[k].reshape(P, TILES) for k in
                          ("r_item_ids", "r_wf1", "r_wf2", "r_category_ids")], axis=1)

    tables = np.zeros((P, T_COLS), f32)
    cat = np.zeros((CAT_SLOTS * CHUNKS * P, CAT), f32)
    cat[:NUM_CATS] = a["L0_rec_cat_emb"]
    tables[:, T_CAT:T_WIDE] = cat.reshape(CAT_SLOTS, CHUNKS, P, CAT).transpose(2, 1, 0, 3).reshape(P, -1)
    for w, name in enumerate(("L0_rec_wide_emb1", "L0_rec_wide_emb2")):
        wide = np.zeros(WIDE_SLOTS * WQ, f32)
        wide[:DIM] = a[name][:, 0]
        tables[w * WQ:(w + 1) * WQ, T_WIDE + w * WIDE_SLOTS:T_WIDE + (w + 1) * WIDE_SLOTS] = \
            wide.reshape(WIDE_SLOTS, WQ).T
    part = np.arange(P)
    for c in range(CHUNKS):
        tables[:, T_QCAT + c] = part + c * P
    tables[:, T_QWIDE] = part % WQ
    tables[:, T_SLOT:T_SLOT + WIDE_SLOTS] = np.arange(WIDE_SLOTS)

    weights = np.zeros((P, W_COLS), f32)
    w1 = a["L0_rec_W1"]
    weights[:USER, W_DIRECT:W_DIRECT + H1] = w1[:USER]
    weights[USER:DIRECT, W_DIRECT:W_DIRECT + H1] = w1[USER + ROWS:]
    weights[:ROWS, W_ROWS:W_ROWS + H1] = w1[USER:USER + ROWS]
    weights[:H1, W_2:W_2 + H2] = a["L0_rec_W2"]
    for k in range(2):
        weights[k * H2:(k + 1) * H2, W_3 + k * H3:W_3 + (k + 1) * H3] = a["L0_rec_W3"]
    for g in range(GROUPS):
        weights[g * H3:(g + 1) * H3, W_4 + g] = a["L0_rec_W4"][:, 0]
    for i, n in enumerate((H1, H2, H3)):
        weights[:, W_G + i] = np.tile(a[f"L0_rec_g{i + 1}"], P // n)
        weights[:, W_B + i] = np.tile(a[f"L0_rec_b{i + 1}"], P // n)
        weights[:, W_BE + i] = np.tile(a[f"L0_rec_be{i + 1}"], P // n)
    weights[:, W_B4] = a["L0_rec_b4"]

    def flip(x):
        return np.ascontiguousarray(x.reshape(P, TILES, -1).transpose(2, 1, 0).reshape(-1, B))

    arrays = {
        "ids": np.ascontiguousarray(ids),
        "tables": tables,
        "weights": weights,
        "user_t": flip(a["r_user_embeddings"]),
        "dense_t": flip(np.concatenate([a["r_price_features"], a["r_temporal_features"]], axis=1)),
        "item_emb": np.ascontiguousarray(a["L0_rec_item_emb"]),
        "cross_w": np.ascontiguousarray(a["L0_rec_cross_W"]).reshape(-1, 1),
    }
    nc = bacc.Bacc("TRN2", target_bir_lowering=False, num_devices=1)
    args = [nc.dram_tensor(k, v.shape, mybir.dt.from_np(v.dtype), kind="ExternalInput").ap()
            for k, v in arrays.items()]
    out = nc.dram_tensor("out", (P, TILES), F32, kind="ExternalOutput").ap()
    wide_deep(nc, *args, out)
    r = run_bass_kernel_spmd(nc, [arrays], core_ids=[0])
    return r.results[0]["out"].reshape(B, 1)
```
